# Optimizing a Trainium2 kernel written in Bass

```python
import numpy as np
import jax
import jax.numpy as jnp

def _softmax(x, axis=-1):
    return jax.nn.softmax(x, axis=axis)

def _gelu(x):
    return jax.nn.gelu(x, approximate=True)

def _silu(x):
    return jax.nn.silu(x)

def _sigmoid(x):
    return jax.nn.sigmoid(x)

def _layernorm(x, axis=-1, eps=1e-05):
    m = jnp.mean(x, axis=axis, keepdims=True)
    v = jnp.var(x, axis=axis, keepdims=True)
    return (x - m) / jnp.sqrt(v + eps)

def _scatter_add(tgt, idx, src, axis=0):
    return tgt.at[idx].add(src)

def _segment_sum(src, seg, n):
    return jax.ops.segment_sum(src, seg, n)
kernel_name = 'mk_rec_standalone_d1_rec_r8_d0d372'

def setup_inputs(seed: int=0):
    np.random.seed(seed)
    _w = jnp.asarray

    def _rec_inputs():
        import jax
        import jax.numpy as jnp
        _rk = jax.random.key(seed)
        r_inputs = 7.22013e-05 + 1.00017 * jax.random.normal(jax.random.fold_in(_rk, 1), (2048, 32, 64), jnp.float32)
        return r_inputs
    r_inputs = _rec_inputs()

    def _L0_rec_setup():
        import jax, jax.numpy as jnp
        import numpy as np
        key = jax.random.key(seed)
        k1, k2 = jax.random.split(key)
        B, F, D = (512, 32, 64)
        P = F * (F - 1) // 2
        inputs = jax.random.normal(k1, (B, F, D), dtype=jnp.float32)
        W = jax.random.normal(k2, (P, D, D), dtype=jnp.float32) * 0.05
        return {'inputs': inputs, 'W': W}
    _L0_rec_all = _L0_rec_setup()
    _L0_rec_in = {k: v for k, v in _L0_rec_all.items() if k in ('W',)}
    del _L0_rec_all
    return {'r_inputs': r_inputs, 'L0_rec_W': _L0_rec_in['W']}

def reference(r_inputs, L0_rec_W):
    import jax
    import jax.numpy as jnp

    def _L0_rec_ref(inputs, W):
        import jax, jax.numpy as jnp
        import numpy as np
        F = inputs.shape[1]
        idx_i, idx_j = np.triu_indices(F, k=1)
        vi = inputs[:, idx_i, :]
        vj = inputs[:, idx_j, :]
        vidots = jnp.einsum('bpd,pde->bpe', vi, W)
        return vidots * vj
    y = _L0_rec_ref(r_inputs, L0_rec_W)
    return y

_drawn_inputs = setup_inputs


def setup_inputs(seed=0):
    import zlib

    import numpy as np

    out = dict(_drawn_inputs(seed))
    spreads = {}
    factors = {}
    for name, (base, spread) in spreads.items():
        noise = np.random.default_rng([zlib.crc32(name.encode()), seed]).standard_normal(out[name].shape)
        drawn = base * np.exp(spread * noise) if base else spread * noise
        out[name] = jnp.asarray(drawn.astype(out[name].dtype))
    for name, factor in factors.items():
        out[name] = (out[name] * factor).astype(out[name].dtype)
    return out
```

```python
import concourse.bass as bass
from concourse import mybir
from contextlib import ExitStack

F = 32
D = 64
PAIRS = F * (F - 1) // 2
BATCH = 2048
ROWS = 128
TILES = BATCH // ROWS
BANK_PAIRS = 512 // D
FILL = 2 * BANK_PAIRS
FILLS = PAIRS // FILL
SLOTS = 4
STORES = 16
CHUNK = PAIRS // STORES
RING = 4
X_BUFS = 2
PARTS = ((0, 8), (8, 16), (16, 24), (24, 28), (28, 32))
RAW_BUFS = 4
SPLIT_LEAD = 3
DOUBLE_LEAD = 3
ROUND_LEAD = 5
TO_SCALAR = (2, 6, 10, 14, 18, 22, 26, 28, 30)

STEADY = ([("products", n) for n in range(0, 4)] + [("transposes", 4)]
          + [("products", n) for n in range(4, 15)] + [("transposes", 0)]
          + [("products", n) for n in range(15, 25)] + [("transposes", 1)]
          + [("products", n) for n in range(25, 30)] + [("transposes", 2)]
          + [("products", 30), ("transposes", 3)])
FIRST = ([("products", n) for n in range(0, 4)] + [("transposes", 4)]
         + [("products", n) for n in range(4, FILLS)] + [("transposes", part) for part in range(4)])
LAST = FIRST[:-4]
BODIES = (TILES - 2) // 2
PER_TILE = len(STEADY)
BEFORE = len(PARTS) - 1

assert FILLS * FILL == PAIRS and CHUNK * STORES == PAIRS and STORES % RING == 0
assert PER_TILE == len(FIRST) and PER_TILE % SLOTS == 0 and BEFORE == SLOTS


def first_pair(i):
    return i * (F - 1) - i * (i - 1) // 2


LEFT = [i for i in range(F) for _ in range(i + 1, F)]


def runs(lo, hi, cuts):
    at, out = lo, []
    while at < hi:
        end = min(hi, first_pair(LEFT[at] + 1), (at // cuts + 1) * cuts)
        out.append((at, end))
        at = end
    return out


def upto(body, half, per_tile, extra):
    return body * (2 * per_tile) + ((half + 1) * per_tile + extra)


def products_in_slot(order, slot, end=PER_TILE):
    return sum(1 for n, (kind, _) in enumerate(order[:end]) if kind == "products" and n % SLOTS == slot)


def freed_count(order, body, half, n):
    slot = n % SLOTS
    steady = products_in_slot(STEADY, slot)
    head = 0 if order is FIRST else products_in_slot(FIRST, slot) - steady
    return upto(body, half, steady, 1 + head + products_in_slot(order, slot, n))


def bilinear_kernel(nc, x, w, y):
    fp32, fp32r = mybir.dt.float32, mybir.dt.float32r
    ALU = mybir.AluOpType

    with ExitStack() as ctx:
        w_sb = ctx.enter_context(nc.sbuf_tensor("w_sb", [ROWS, PAIRS * D], fp32r))
        xh_t = ctx.enter_context(nc.sbuf_tensor("xh_t", [ROWS, F, ROWS], fp32r))
        xl_t = ctx.enter_context(nc.sbuf_tensor("xl_t", [ROWS, F, ROWS], fp32r))
        x_sb = ctx.enter_context(nc.sbuf_tensor("x_sb", [ROWS, X_BUFS, F * D], fp32))
        ring = ctx.enter_context(nc.sbuf_tensor("ring", [ROWS, RING * CHUNK * D], fp32))
        x_twice = ctx.enter_context(nc.sbuf_tensor("x_twice", [ROWS, 8, 2, D], fp32))
        ident = ctx.enter_context(nc.sbuf_tensor("ident", [ROWS, ROWS], fp32))
        psum = ctx.enter_context(nc.psum_tensor("psum", [ROWS, SLOTS, FILL * D], fp32))

        def sem(name):
            return ctx.enter_context(nc.semaphore(name))

        x_loaded = [sem(f"x_loaded{b}") for b in range(X_BUFS)]
        w_loaded = [sem(f"w_loaded{b}") for b in range(RAW_BUFS)]
        ident_zero = sem("ident_zero")
        ident_ready = sem("ident_ready")
        w_rounded = sem("w_rounded")
        w_split = sem("w_split")
        x_doubled = sem("x_doubled")
        x_rounded = sem("x_rounded")
        x_split = sem("x_split")
        filled = sem("filled")
        freed = [sem(f"freed{s}") for s in range(SLOTS)]
        multiplied = sem("multiplied")
        stored = [sem(f"stored{r}") for r in range(RING)]
        block = ctx.enter_context(nc.Block())

        def raw(c):
            b = c % RAW_BUFS
            return x_sb[:, 1, b * FILL * D // 2:(b + 1) * FILL * D // 2]

        def in_ring(lo, hi):
            at = lo % (RING * CHUNK) * D
            return ring[:, at:at + (hi - lo) * D]

        def in_psum(slot, lo, hi):
            at = lo % FILL * D
            return psum[:, slot, at:at + (hi - lo) * D]

        def right_factors(buf, lo, hi):
            j = lo - first_pair(LEFT[lo]) + LEFT[lo] + 1
            return x_sb[:, buf, j * D:(j + hi - lo) * D]

        def new_chunks(lo, hi):
            return [c for c in range(STORES) if lo <= c * CHUNK < hi]

        def ring_count(body, half, c):
            return upto(body, half, 16 * STORES // RING, 16 * (c // RING + 1))

        def parts_count(body, half, part):
            return upto(body, half, len(PARTS), part + 1 + (0 if part == 4 else len(PARTS)))

        @block.sync
        def _(sp):
            def load_w(c):
                sp.dma_start(raw(c), w[:, c * FILL * D // 2:(c + 1) * FILL * D // 2]).then_inc(w_loaded[c % RAW_BUFS], 16)

            def stores(order, body, half):
                pieces = RAW_BUFS
                for c in range(STORES):
                    last = ((c + 1) * CHUNK - 1) // FILL
                    while order is FIRST and pieces < min(FILLS, last + 1 + 2 * SPLIT_LEAD):
                        sp.wait_ge(w_split, pieces - RAW_BUFS + 1)
                        load_w(pieces)
                        pieces += 1
                    by_vector = order.index(("products", max(n for n in range(last + 1) if n not in TO_SCALAR)))
                    vector_count = freed_count(order, body, half, by_vector) + 1
                    gpsimd_count = upto(body, half, len(TO_SCALAR), sum(n <= last for n in TO_SCALAR))
                    sp.compute_val(vector_count)
                    sp.compute_val(gpsimd_count)
                    sp.compute_val(((body * 2 + (half + 1)) * (ROWS * PAIRS * D) + c * CHUNK * D) * 4)
                    sp.wait_ge(freed[by_vector % SLOTS], vector_count)
                    if order is not FIRST or last >= min(TO_SCALAR):
                        sp.wait_ge(multiplied, gpsimd_count)
                    sp.dma_start(y[body * 2 + (half + 1), c, :, :],
                                 in_ring(c * CHUNK, (c + 1) * CHUNK)).then_inc(stored[c % RING], 16)
                    if order is FIRST and c == STORES - 3:
                        sp.wait_ge(w_split, FILLS)
                        sp.dma_start(x_sb[:, 1, :], x[1, :, :]).then_inc(x_loaded[1], 16)

            def load_x(body, half):
                buf = (half + 1) % X_BUFS
                sp.dma_start(x_sb[:, buf, :], x[body * 2 + (half + 3), :, :]).then_inc(x_loaded[buf], 16)

            sp.dma_start(x_sb[:, 0, :], x[0, :, :]).then_inc(x_loaded[0], 16)
            for c in range(RAW_BUFS):
                load_w(c)
            for r in range(RING):
                sp.sem_inc(stored[r], 16)
            stores(FIRST, 0, -1)
            load_x(0, -1)
            with sp.Fori(0, BODIES - 1) as body:
                for half in range(2):
                    stores(STEADY, body, half)
                    load_x(body, half)
            stores(STEADY, BODIES - 1, 0)
            load_x(BODIES - 1, 0)
            stores(STEADY, BODIES - 1, 1)
            stores(LAST, BODIES, 0)
            for r in range(RING):
                sp.wait_ge(stored[r], 16 * (TILES * STORES // RING + 1))

        @block.tensor
        def _(pe):
            def transposes(slot, part):
                for at in range(PARTS[part][1] - PARTS[part][0]):
                    last = nc.tensor.transpose(psum[:, slot, at * ROWS:(at + 1) * ROWS],
                                               x_twice[:, at, :, :].rearrange("p a d -> p (a d)"), ident[:, :])
                last.then_inc(filled, 1)

            def products(slot, fill):
                for lo, hi in runs(fill * FILL, (fill + 1) * FILL, BANK_PAIRS):
                    nc.tensor.matmul(in_psum(slot, lo, hi), xh_t[:, LEFT[lo], :], w_sb[:, lo * D:hi * D],
                                     start=True, stop=False)
                    last = nc.tensor.matmul(in_psum(slot, lo, hi), xl_t[:, LEFT[lo], :], w_sb[:, lo * D:hi * D],
                                            start=False, stop=True)
                last.then_inc(filled, 1)

            def fills(order, body, half):
                has_split = 0
                for n, (kind, which) in enumerate(order):
                    slot = n % SLOTS
                    free_at = freed_count(order, body, half, n)
                    pe.compute_val(free_at)
                    if kind == "transposes":
                        doubled_at = parts_count(body, half, which)
                        pe.compute_val(doubled_at)
                        pe.wait_ge(x_doubled, doubled_at)
                        pe.wait_ge(freed[slot], free_at)
                        transposes(slot, which)
                        continue
                    needs = [part + 1 for part, (f, _) in enumerate(PARTS) if f <= LEFT[(which + 1) * FILL - 1]]
                    if n >= SLOTS and order[n - SLOTS][0] == "transposes":
                        part = order[n - SLOTS][1]
                        needs.append(part + 1 + (0 if part == 4 else len(PARTS)))
                    if n in (1, 3):
                        needs.append(n // 2 + 3)
                    if max(needs) > has_split:
                        has_split = max(needs)
                        split_at = upto(body, half, len(PARTS), has_split)
                        pe.compute_val(split_at)
                        pe.wait_ge(x_split, split_at)
                    if order is FIRST:
                        pe.wait_ge(w_split, which + 1)
                    pe.wait_ge(freed[slot], free_at)
                    products(slot, which)

            for slot in range(SLOTS):
                pe.sem_inc(freed[slot], 1)
            pe.wait_ge(ident_ready, 1)
            for part in range(BEFORE):
                pe.wait_ge(x_doubled, part + 1)
                transposes(part, part)
            fills(FIRST, 0, -1)
            with pe.Fori(0, BODIES) as body:
                for half in range(2):
                    fills(STEADY, body, half)
            fills(LAST, BODIES, 0)

        @block.scalar
        def _(act):
            def round_w(c):
                act.wait_ge(w_loaded[c % RAW_BUFS], 16 * (c // RAW_BUFS + 1))
                for h in range(2):
                    rows, col = slice(h * D, (h + 1) * D), (c * FILL + h * FILL // 2) * D
                    last = nc.scalar.copy(w_sb[rows, col:col + FILL * D // 2], raw(c)[rows, :])
                last.then_inc(w_rounded, 1)

            def double_x(body, half, part):
                lo, hi = PARTS[part]
                tile = half + 1 + (part != 4)
                loaded_at = body * 16 + 16 * (1 + tile // 2)
                act.compute_val(loaded_at)
                act.wait_ge(x_loaded[tile % X_BUFS], loaded_at)
                once = x_sb[:, tile % X_BUFS, lo * D:hi * D].rearrange("p (f d) -> p f d", d=D)
                nc.scalar.copy(x_twice[:, 0:hi - lo, :, :],
                               once.unsqueeze(2).broadcast_to([ROWS, hi - lo, 2, D])).then_inc(x_doubled, 1)

            def round_x(slot, part):
                lo, hi = PARTS[part]
                nc.scalar.copy(xh_t[:, lo:hi, :], psum[:, slot, 0:(hi - lo) * ROWS]).then_inc(x_rounded, 1)

            def drains(order, body, half):
                seen, doubled = set(), []
                for n, (kind, which) in enumerate(order):
                    if order is FIRST and kind == "products" and which + ROUND_LEAD < FILLS:
                        round_w(which + ROUND_LEAD)
                    for ahead in range(n, min(n + DOUBLE_LEAD, len(order) - 1) + 1):
                        if order[ahead][0] == "transposes" and order[ahead] not in doubled \
                                and not any(k == "transposes" for k, _ in order[n:ahead]):
                            doubled.append(order[ahead])
                            double_x(body, half, order[ahead][1])
                    if kind == "products" and which not in TO_SCALAR:
                        continue
                    filled_at = upto(body, half, PER_TILE, BEFORE + n + 1)
                    act.compute_val(filled_at)
                    if kind == "transposes":
                        act.wait_ge(filled, filled_at)
                        round_x(n % SLOTS, which)
                        continue
                    act.wait_ge(filled, filled_at)
                    lo, end = which * FILL, (which + 1) * FILL
                    while lo < end:
                        hi = min(end, (lo // (RING * CHUNK) + 1) * (RING * CHUNK))
                        for c in range(lo // CHUNK, (hi - 1) // CHUNK + 1):
                            if c not in seen:
                                seen.add(c)
                                free_at = ring_count(body, half, c)
                                act.compute_val(free_at)
                                act.wait_ge(stored[c % RING], free_at)
                        last = nc.scalar.copy(in_ring(lo, hi), in_psum(n % SLOTS, lo, hi))
                        lo = hi
                    last.then_inc(freed[n % SLOTS], 1)

            for part in range(BEFORE):
                double_x(0, -2, part)
                round_w(part)
                act.wait_ge(filled, part + 1)
                round_x(part, part)
            for c in range(BEFORE, ROUND_LEAD):
                round_w(c)
            drains(FIRST, 0, -1)
            with act.Fori(0, BODIES) as body:
                for half in range(2):
                    drains(STEADY, body, half)
            drains(LAST, BODIES, 0)

        @block.vector
        def _(dve):
            def split_w(c):
                dve.wait_ge(w_rounded, c + 1)
                for h in range(2):
                    rows, other = slice(h * D, (h + 1) * D), slice((1 - h) * D, (2 - h) * D)
                    col = (c * FILL + h * FILL // 2) * D
                    last = nc.vector.tensor_tensor(w_sb[other, col:col + FILL * D // 2], raw(c)[rows, :],
                                                   w_sb[rows, col:col + FILL * D // 2], ALU.subtract)
                last.then_inc(w_split, 1)

            def split_x(slot, part):
                lo, hi = PARTS[part]
                nc.vector.tensor_tensor(xl_t[:, lo:hi, :], psum[:, slot, 0:(hi - lo) * ROWS], xh_t[:, lo:hi, :],
                                        ALU.subtract).then_inc(x_split, 1)

            def drains(order, body, half):
                seen = set()
                for n, (kind, which) in enumerate(order):
                    if order is FIRST and kind == "products" and which + SPLIT_LEAD < FILLS:
                        split_w(which + SPLIT_LEAD)
                    if kind == "transposes":
                        rounded_at = parts_count(body, half, which)
                        dve.compute_val(rounded_at)
                        dve.wait_ge(x_rounded, rounded_at)
                        split_x(n % SLOTS, which)
                    elif which not in TO_SCALAR:
                        filled_at = upto(body, half, PER_TILE, BEFORE + n + 1)
                        dve.compute_val(filled_at)
                        dve.wait_ge(filled, filled_at)
                        for lo, hi in runs(which * FILL, (which + 1) * FILL, RING * CHUNK):
                            for c in range(lo // CHUNK, (hi - 1) // CHUNK + 1):
                                if c not in seen:
                                    seen.add(c)
                                    free_at = ring_count(body, half, c)
                                    dve.compute_val(free_at)
                                    dve.wait_ge(stored[c % RING], free_at)
                            last = nc.vector.tensor_tensor(in_ring(lo, hi), in_psum(n % SLOTS, lo, hi),
                                                           right_factors((half + 1) % X_BUFS, lo, hi), ALU.mult)
                        last.then_inc(freed[n % SLOTS], 1)

            for part in range(BEFORE):
                dve.wait_ge(x_rounded, part + 1)
                split_x(part, part)
                if part < SPLIT_LEAD:
                    split_w(part)
            drains(FIRST, 0, -1)
            with dve.Fori(0, BODIES) as body:
                for half in range(2):
                    drains(STEADY, body, half)
            drains(LAST, BODIES, 0)

        @block.gpsimd
        def _(pool):
            nc.gpsimd.memset(ident[:, :], 0.0).then_inc(ident_zero, 1)
            pool.wait_ge(ident_zero, 1)
            nc.gpsimd.affine_select(out=ident[:, :], in_=ident[:, :], compare_op=ALU.not_equal, fill=1.0,
                                    base=0, pattern=[[-1, ROWS]], channel_multiplier=1).then_inc(ident_ready, 1)

            def multiplies(order, body, half):
                for fill in TO_SCALAR:
                    n = order.index(("products", fill))
                    copied_at = freed_count(order, body, half, n) + 1
                    pool.compute_val(copied_at)
                    pool.wait_ge(freed[n % SLOTS], copied_at)
                    for lo, hi in runs(fill * FILL, (fill + 1) * FILL, RING * CHUNK):
                        last = nc.gpsimd.tensor_tensor(in_ring(lo, hi), in_ring(lo, hi),
                                                       right_factors((half + 1) % X_BUFS, lo, hi), ALU.mult)
                    last.then_inc(multiplied, 1)

            multiplies(FIRST, 0, -1)
            with pool.Fori(0, BODIES) as body:
                for half in range(2):
                    multiplies(STEADY, body, half)
            multiplies(LAST, BODIES, 0)


def kernel(r_inputs, L0_rec_W):
    import numpy as np
    import concourse.bacc as bacc
    from concourse.bass_utils import run_bass_kernel_spmd

    x = np.ascontiguousarray(r_inputs).reshape(TILES, ROWS, F * D)
    w = np.asarray(L0_rec_W).reshape(FILLS, 2, FILL // 2, D, D).transpose(1, 3, 0, 2, 4)
    arrays = {"x": x, "w": np.ascontiguousarray(w).reshape(ROWS, PAIRS * D // 2)}

    nc = bacc.Bacc("TRN2", target_bir_lowering=False, num_devices=1)
    fp32 = mybir.dt.float32
    aps = [nc.dram_tensor(name, a.shape, fp32, kind="ExternalInput").ap() for name, a in arrays.items()]
    y = nc.dram_tensor("y", (BATCH, PAIRS * D), fp32, kind="ExternalOutput").ap()
    bilinear_kernel(nc, *aps, y.rearrange("(t p) (c e) -> t c p e", p=ROWS, c=STORES))
    r = run_bass_kernel_spmd(nc, [arrays], core_ids=[0])
    return r.results[0]["y"].reshape(BATCH, PAIRS, D)
```

```python
import concourse.bass as bass
from concourse import mybir
from contextlib import ExitStack

F = 32
D = 64
PAIRS = F * (F - 1) // 2
BATCH = 2048
ROWS = 128
TILES = BATCH // ROWS
BANK_PAIRS = 512 // D
FILL = 2 * BANK_PAIRS
FILLS = PAIRS // FILL
PIECE = FILL * D // 2
SLOTS = 4
STORES = 16
CHUNK = PAIRS // STORES
RING = 4
X_BUFS = 2
DOUBLE_LEAD = 3
W_GROUPS = (0, 2, 6, 12, 16, 20, 24, 28, FILLS - 1, FILLS)
ROUND_LEAD, SPLIT_LEAD = 4, 3
W_AFTER = (1, 3, 5, 7, 7)
X_AFTER = 4


def products(lo, hi):
    return [("products", n) for n in range(lo, hi)]


STEADY = (products(0, 4) + [("own", (20, 28))] + products(4, 9) + [("own", (28, 32))] + products(9, 15)
          + [("next", (0, 8))] + products(15, 24) + [("next", (8, 16))] + products(24, 27)
          + [("next", (16, 20))] + products(27, 31))
FIRST = ([("own", (0, 4))] + products(0, 3) + [("own", (4, 8))] + products(3, 7) + [("own", (8, 16))]
         + products(7, 11) + [("own", (16, 20))] + products(11, 19)
         + [("own", (20, 28))] + products(19, 22) + [("next", (0, 8))] + products(22, 25) + [("next", (8, 16))]
         + products(25, 26) + [("own", (28, 32))] + products(26, 27) + [("next", (16, 20))] + products(27, 31))
NEXT = [part for kind, part in STEADY if kind == "next"]
W_LAST_IN = ("own", (28, 32))
LAST = [fill for fill in STEADY if fill[0] != "next"]
BODIES = (TILES - 2) // 2

TO_SCALAR = (2, 6, 10, 14, 18, 22, 26, 28, 30)
FIRST_TO_SCALAR = (3, 6, 9, 12, 15, 17, 19, 21, 23, 25, 28, 30)

assert FILLS * FILL == PAIRS and CHUNK * STORES == PAIRS and STORES % RING == 0
assert len(STEADY) % SLOTS == 0 and len(FIRST) % SLOTS == 0 and STEADY[-SLOTS:] == FIRST[-SLOTS:]


def first_pair(i):
    return i * (F - 1) - i * (i - 1) // 2


LEFT = [i for i in range(F) for _ in range(i + 1, F)]


def runs(lo, hi, cuts):
    at, out = lo, []
    while at < hi:
        end = min(hi, first_pair(LEFT[at] + 1), (at // cuts + 1) * cuts)
        out.append((at, end))
        at = end
    return out


def upto(body, half, per_tile, extra):
    return body * (2 * per_tile) + ((half + 1) * per_tile + extra)


def counted(order, body, half, per_tile, in_first, n):
    return upto(body, half, per_tile, n + (0 if order is FIRST else in_first - per_tile))


def fill_count(order, body, half, n):
    return counted(order, body, half, len(STEADY), len(FIRST), n + 1)


def parts_in(order, end=None):
    return sum(kind != "products" for kind, _ in order[:end])


def part_count(order, body, half, n):
    return counted(order, body, half, parts_in(STEADY), parts_in(FIRST), parts_in(order, n + 1))


def products_in_slot(order, slot, end=None):
    return sum(kind == "products" and n % SLOTS == slot for n, (kind, _) in enumerate(order[:end]))


def freed_count(order, body, half, n):
    slot = n % SLOTS
    return counted(order, body, half, products_in_slot(STEADY, slot), products_in_slot(FIRST, slot),
                   1 + products_in_slot(order, slot, n))


def split_needed(order, n):
    kind, which = order[n]
    needed = []
    if kind == "products":
        last_left = LEFT[(which + 1) * FILL - 1]
        own = [m for m, (k, part) in enumerate(order) if k == "own" and part[0] <= last_left]
        if own:
            needed.append(parts_in(order, own[-1] + 1))
        if order is not FIRST and last_left < NEXT[-1][1]:
            needed.append(1 - sum(last_left < hi for _, hi in NEXT))
    before = n - SLOTS
    if before >= 0 and order[before][0] != "products":
        needed.append(parts_in(order, before + 1))
    if before < 0 and order is not FIRST and STEADY[before][0] != "products":
        needed.append(parts_in(STEADY[:before]) + 1 - parts_in(STEADY))
    return max(needed, default=None)


def scalar_fills(order):
    return FIRST_TO_SCALAR if order is FIRST else TO_SCALAR


def pieces_before(fill, lead):
    return min(FILLS, fill + lead + fill // 6)


def bilinear_kernel(nc, x, w, y):
    fp32, fp32r = mybir.dt.float32, mybir.dt.float32r
    ALU = mybir.AluOpType

    with ExitStack() as ctx:
        place = (nc.sbuf_base + 63) // 64 * 64

        def sbuf(name, shape, dtype, at=None):
            nonlocal place
            if at is not None:
                return nc.alloc_sbuf_tensor_at(name, shape, dtype, offset=at)
            size = 4
            for n in shape[1:]:
                size *= n
            place += size
            return nc.alloc_sbuf_tensor_at(name, shape, dtype, offset=place - size)

        w_at = place
        w_sb = sbuf("w_sb", [ROWS, PAIRS * D], fp32r)
        xh_t = sbuf("xh_t", [ROWS, F, ROWS], fp32r)
        xh_end = place
        xl_t = sbuf("xl_t", [ROWS, F, ROWS], fp32r)
        x_sb = sbuf("x_sb", [ROWS, X_BUFS, F * D], fp32)
        ring = sbuf("ring", [ROWS, RING * CHUNK * D], fp32)
        x_twice = sbuf("x_twice", [ROWS, 8, 2, D], fp32)
        ident = sbuf("ident", [ROWS, ROWS], fp32)
        w_raw = sbuf("w_raw", [ROWS, (FILLS - 1) * PIECE], fp32, at=w_at + (PAIRS * D - (FILLS - 1) * PIECE) * 4)
        w_raw_last = sbuf("w_raw_last", [ROWS, PIECE], fp32, at=xh_end - PIECE * 4)
        psum = ctx.enter_context(nc.psum_tensor("psum", [ROWS, SLOTS, FILL * D], fp32))

        def sem(name):
            return ctx.enter_context(nc.semaphore(name))

        x_loaded = [sem(f"x_loaded{b}") for b in range(X_BUFS)]
        x_head_loaded = sem("x_head_loaded")
        w_loaded = [sem(f"w_loaded{g}") for g in range(len(W_GROUPS) - 1)]
        ident_zero = sem("ident_zero")
        ident_ready = sem("ident_ready")
        w_rounded = sem("w_rounded")
        w_split = sem("w_split")
        x_doubled = sem("x_doubled")
        x_rounded = sem("x_rounded")
        x_split = sem("x_split")
        filled = sem("filled")
        freed = [sem(f"freed{s}") for s in range(SLOTS)]
        multiplied = sem("multiplied")
        stored = [sem(f"stored{r}") for r in range(RING)]
        block = ctx.enter_context(nc.Block())

        def raw(c):
            return w_raw[:, c * PIECE:(c + 1) * PIECE] if c < FILLS - 1 else w_raw_last[:, :]

        def in_ring(lo, hi):
            at = lo % (RING * CHUNK) * D
            return ring[:, at:at + (hi - lo) * D]

        def in_psum(slot, lo, hi):
            at = lo % FILL * D
            return psum[:, slot, at:at + (hi - lo) * D]

        def right_factors(buf, lo, hi):
            j = lo - first_pair(LEFT[lo]) + LEFT[lo] + 1
            return x_sb[:, buf, j * D:(j + hi - lo) * D]

        def ring_count(body, half, c):
            return upto(body, half, 16 * STORES // RING, 16 * (c // RING + 1))

        @block.sync
        def _(sp):
            def load_w(g):
                lo, hi = W_GROUPS[g] * PIECE, W_GROUPS[g + 1] * PIECE
                to = w_raw[:, lo:hi] if W_GROUPS[g] < FILLS - 1 else w_raw_last[:, :]
                sp.dma_start(to, w[:, lo:hi]).then_inc(w_loaded[g], 16)

            def stores(order, body, half):
                theirs = scalar_fills(order)
                for c in range(STORES):
                    last = ((c + 1) * CHUNK - 1) // FILL
                    by_vector = order.index(("products", max(n for n in range(last + 1) if n not in theirs)))
                    vector_count = freed_count(order, body, half, by_vector) + 1
                    gpsimd_count = counted(order, body, half, len(TO_SCALAR), len(FIRST_TO_SCALAR),
                                           sum(n <= last for n in theirs))
                    sp.compute_val(vector_count)
                    sp.compute_val(gpsimd_count)
                    sp.compute_val(((body * 2 + (half + 1)) * (ROWS * PAIRS * D) + c * CHUNK * D) * 4)
                    sp.wait_ge(freed[by_vector % SLOTS], vector_count)
                    if order is not FIRST or last >= min(theirs):
                        sp.wait_ge(multiplied, gpsimd_count)
                    sp.dma_start(y[body * 2 + (half + 1), c, :, :],
                                 in_ring(c * CHUNK, (c + 1) * CHUNK)).then_inc(stored[c % RING], 16)
                    if order is FIRST:
                        for g, after in enumerate(W_AFTER, len(w_loaded) - len(W_AFTER)):
                            if c == after:
                                load_w(g)
                    if order is FIRST and c == X_AFTER:
                        sp.dma_start(x_sb[:, 1, :], x[1, :, :]).then_inc(x_loaded[1], 16)

            def load_x(body, half):
                buf = (half + 1) % X_BUFS
                sp.dma_start(x_sb[:, buf, :], x[body * 2 + (half + 3), :, :]).then_inc(x_loaded[buf], 16)

            head = FIRST[0][1][1] * D
            sp.dma_start(x_sb[:, 0, 0:head], x[0, :, 0:head]).then_inc(x_head_loaded, 16)
            load_w(0)
            sp.dma_start(x_sb[:, 0, head:], x[0, :, head:]).then_inc(x_loaded[0], 16)
            for g in range(1, len(w_loaded) - len(W_AFTER)):
                load_w(g)
            for r in range(RING):
                sp.sem_inc(stored[r], 16)
            stores(FIRST, 0, -1)
            load_x(0, -1)
            with sp.Fori(0, BODIES - 1) as body:
                for half in range(2):
                    stores(STEADY, body, half)
                    load_x(body, half)
            stores(STEADY, BODIES - 1, 0)
            load_x(BODIES - 1, 0)
            stores(STEADY, BODIES - 1, 1)
            stores(LAST, BODIES, 0)
            for r in range(RING):
                sp.wait_ge(stored[r], 16 * (TILES * STORES // RING + 1))

        @block.tensor
        def _(pe):
            def transposes(slot, part):
                for at in range(part[1] - part[0]):
                    last = nc.tensor.transpose(psum[:, slot, at * ROWS:(at + 1) * ROWS],
                                               x_twice[:, at, :, :].rearrange("p a d -> p (a d)"), ident[:, :])
                last.then_inc(filled, 1)

            def multiply(slot, fill):
                for lo, hi in runs(fill * FILL, (fill + 1) * FILL, BANK_PAIRS):
                    nc.tensor.matmul(in_psum(slot, lo, hi), xh_t[:, LEFT[lo], :], w_sb[:, lo * D:hi * D],
                                     start=True, stop=False)
                    last = nc.tensor.matmul(in_psum(slot, lo, hi), xl_t[:, LEFT[lo], :], w_sb[:, lo * D:hi * D],
                                            start=False, stop=True)
                last.then_inc(filled, 1)

            def fills(order, body, half):
                split = -len(STEADY)
                for n, (kind, which) in enumerate(order):
                    slot = n % SLOTS
                    free_at = freed_count(order, body, half, n)
                    pe.compute_val(free_at)
                    needed = split_needed(order, n)
                    if needed is not None and needed > split:
                        split = needed
                        split_at = counted(order, body, half, parts_in(STEADY), parts_in(FIRST), split)
                        pe.compute_val(split_at)
                    else:
                        needed = None
                    if kind != "products":
                        doubled_at = part_count(order, body, half, n)
                        pe.compute_val(doubled_at)
                        pe.wait_ge(x_doubled, doubled_at)
                    elif order is FIRST:
                        pe.wait_ge(w_split, which + 1)
                    if needed is not None:
                        pe.wait_ge(x_split, split_at)
                    pe.wait_ge(freed[slot], free_at)
                    if kind == "products":
                        multiply(slot, which)
                    else:
                        transposes(slot, which)

            for slot in range(SLOTS):
                pe.sem_inc(freed[slot], 1)
            pe.wait_ge(ident_ready, 1)
            fills(FIRST, 0, -1)
            with pe.Fori(0, BODIES) as body:
                for half in range(2):
                    fills(STEADY, body, half)
            fills(LAST, BODIES, 0)

        @block.scalar
        def _(act):
            def round_w(c):
                group = max(g for g in range(len(w_loaded)) if W_GROUPS[g] <= c)
                if c == W_GROUPS[group]:
                    act.wait_ge(w_loaded[group], 16)
                overwritten = (c + 1) * 2 - (PAIRS * D // PIECE - (FILLS - 1))
                if overwritten > 0:
                    act.wait_ge(w_split, overwritten)
                for h in range(2):
                    rows, col = slice(h * D, (h + 1) * D), c * FILL * D + h * PIECE
                    last = nc.scalar.copy(w_sb[rows, col:col + PIECE], raw(c)[rows, :])
                last.then_inc(w_rounded, 1)

            def double_x(order, body, half, n):
                kind, (lo, hi) = order[n]
                tile = half + 1 + (kind == "next")
                if order is FIRST and n == 0:
                    act.wait_ge(x_head_loaded, 16)
                else:
                    loaded_at = body * 16 + 16 * (1 + tile // 2)
                    act.compute_val(loaded_at)
                    act.wait_ge(x_loaded[tile % X_BUFS], loaded_at)
                once = x_sb[:, tile % X_BUFS, lo * D:hi * D].rearrange("p (f d) -> p f d", d=D)
                nc.scalar.copy(x_twice[:, 0:hi - lo, :, :],
                               once.unsqueeze(2).broadcast_to([ROWS, hi - lo, 2, D])).then_inc(x_doubled, 1)

            def copy_fill(order, body, half, n, waited):
                lo, end = order[n][1] * FILL, (order[n][1] + 1) * FILL
                while lo < end:
                    hi = min(end, (lo // (RING * CHUNK) + 1) * (RING * CHUNK))
                    for c in range(lo // CHUNK, (hi - 1) // CHUNK + 1):
                        if c not in waited:
                            waited.add(c)
                            free_at = ring_count(body, half, c)
                            act.compute_val(free_at)
                            act.wait_ge(stored[c % RING], free_at)
                    last = nc.scalar.copy(in_ring(lo, hi), in_psum(n % SLOTS, lo, hi))
                    lo = hi
                last.then_inc(freed[n % SLOTS], 1)

            def drains(order, body, half):
                waited, doubled, pieces = set(), -1, 0
                for n, (kind, which) in enumerate(order):
                    for ahead in range(n, min(n + DOUBLE_LEAD + 1, len(order))):
                        if order[ahead][0] != "products":
                            if ahead > doubled:
                                doubled = ahead
                                double_x(order, body, half, ahead)
                            break
                    while order is FIRST and kind == "products" and pieces < pieces_before(which, ROUND_LEAD):
                        round_w(pieces)
                        pieces += 1
                    if kind == "products" and which not in scalar_fills(order):
                        continue
                    filled_at = fill_count(order, body, half, n)
                    act.compute_val(filled_at)
                    if kind == "products":
                        act.wait_ge(filled, filled_at)
                        copy_fill(order, body, half, n, waited)
                    else:
                        if order is FIRST and (kind, which) == W_LAST_IN:
                            act.wait_ge(w_split, FILLS)
                        lo, hi = which
                        act.wait_ge(filled, filled_at)
                        nc.scalar.copy(xh_t[:, lo:hi, :], psum[:, n % SLOTS, 0:(hi - lo) * ROWS]).then_inc(x_rounded, 1)

            drains(FIRST, 0, -1)
            with act.Fori(0, BODIES) as body:
                for half in range(2):
                    drains(STEADY, body, half)
            drains(LAST, BODIES, 0)

        @block.vector
        def _(dve):
            def split_w(c):
                dve.wait_ge(w_rounded, c + 1)
                for h in range(2):
                    rows, other = slice(h * D, (h + 1) * D), slice((1 - h) * D, (2 - h) * D)
                    col = c * FILL * D + h * PIECE
                    last = nc.vector.tensor_tensor(w_sb[other, col:col + PIECE], raw(c)[rows, :],
                                                   w_sb[rows, col:col + PIECE], ALU.subtract)
                last.then_inc(w_split, 1)

            def drains(order, body, half):
                waited, pieces = set(), 0
                for n, (kind, which) in enumerate(order):
                    while order is FIRST and kind == "products" and pieces < pieces_before(which, SPLIT_LEAD):
                        split_w(pieces)
                        pieces += 1
                    if kind != "products":
                        lo, hi = which
                        rounded_at = part_count(order, body, half, n)
                        dve.compute_val(rounded_at)
                        dve.wait_ge(x_rounded, rounded_at)
                        nc.vector.tensor_tensor(xl_t[:, lo:hi, :], psum[:, n % SLOTS, 0:(hi - lo) * ROWS],
                                                xh_t[:, lo:hi, :], ALU.subtract).then_inc(x_split, 1)
                    elif which not in scalar_fills(order):
                        filled_at = fill_count(order, body, half, n)
                        dve.compute_val(filled_at)
                        dve.wait_ge(filled, filled_at)
                        for lo, hi in runs(which * FILL, (which + 1) * FILL, RING * CHUNK):
                            for c in range(lo // CHUNK, (hi - 1) // CHUNK + 1):
                                if c not in waited:
                                    waited.add(c)
                                    free_at = ring_count(body, half, c)
                                    dve.compute_val(free_at)
                                    dve.wait_ge(stored[c % RING], free_at)
                            last = nc.vector.tensor_tensor(in_ring(lo, hi), in_psum(n % SLOTS, lo, hi),
                                                           right_factors((half + 1) % X_BUFS, lo, hi), ALU.mult)
                        last.then_inc(freed[n % SLOTS], 1)

            drains(FIRST, 0, -1)
            with dve.Fori(0, BODIES) as body:
                for half in range(2):
                    drains(STEADY, body, half)
            drains(LAST, BODIES, 0)

        @block.gpsimd
        def _(pool):
            nc.gpsimd.memset(ident[:, :], 0.0).then_inc(ident_zero, 1)
            pool.wait_ge(ident_zero, 1)
            nc.gpsimd.affine_select(out=ident[:, :], in_=ident[:, :], compare_op=ALU.not_equal, fill=1.0,
                                    base=0, pattern=[[-1, ROWS]], channel_multiplier=1).then_inc(ident_ready, 1)

            def multiplies(order, body, half):
                for fill in scalar_fills(order):
                    n = order.index(("products", fill))
                    copied_at = freed_count(order, body, half, n) + 1
                    pool.compute_val(copied_at)
                    pool.wait_ge(freed[n % SLOTS], copied_at)
                    for lo, hi in runs(fill * FILL, (fill + 1) * FILL, RING * CHUNK):
                        last = nc.gpsimd.tensor_tensor(in_ring(lo, hi), in_ring(lo, hi),
                                                       right_factors((half + 1) % X_BUFS, lo, hi), ALU.mult)
                    last.then_inc(multiplied, 1)

            multiplies(FIRST, 0, -1)
            with pool.Fori(0, BODIES) as body:
                for half in range(2):
                    multiplies(STEADY, body, half)
            multiplies(LAST, BODIES, 0)


def kernel(r_inputs, L0_rec_W):
    import numpy as np
    import concourse.bacc as bacc
    from concourse.bass_utils import run_bass_kernel_spmd

    x = np.ascontiguousarray(r_inputs).reshape(TILES, ROWS, F * D)
    w = np.asarray(L0_rec_W).reshape(FILLS, 2, FILL // 2, D, D).transpose(1, 3, 0, 2, 4)
    arrays = {"x": x, "w": np.ascontiguousarray(w).reshape(ROWS, PAIRS * D // 2)}

    nc = bacc.Bacc("TRN2", target_bir_lowering=False, num_devices=1)
    fp32 = mybir.dt.float32
    aps = [nc.dram_tensor(name, a.shape, fp32, kind="ExternalInput").ap() for name, a in arrays.items()]
    y = nc.dram_tensor("y", (BATCH, PAIRS * D), fp32, kind="ExternalOutput").ap()
    bilinear_kernel(nc, *aps, y.rearrange("(t p) (c e) -> t c p e", p=ROWS, c=STORES))
    r = run_bass_kernel_spmd(nc, [arrays], core_ids=[0])
    return r.results[0]["y"].reshape(BATCH, PAIRS, D)
```
